# Optimizing a Trainium2 kernel written in Bass

```python
import numpy as np
import jax
import jax.numpy as jnp

def _softmax(x, axis=-1):
    return jax.nn.softmax(x, axis=axis)

def _gelu(x):
    return jax.nn.gelu(x, approximate=True)

def _silu(x):
    return jax.nn.silu(x)

def _sigmoid(x):
    return jax.nn.sigmoid(x)

def _layernorm(x, axis=-1, eps=1e-05):
    m = jnp.mean(x, axis=axis, keepdims=True)
    v = jnp.var(x, axis=axis, keepdims=True)
    return (x - m) / jnp.sqrt(v + eps)

def _scatter_add(tgt, idx, src, axis=0):
    return tgt.at[idx].add(src)

def _segment_sum(src, seg, n):
    return jax.ops.segment_sum(src, seg, n)
kernel_name = 'mk_cond_resid_d1_seqx_r2_73e926'

def setup_inputs(seed: int=0):
    np.random.seed(seed)
    _w = jnp.asarray

    def _rec_inputs():
        import jax
        import jax.numpy as jnp
        _rk = jax.random.key(seed)
        x = 0.0001044 + 1 * jax.random.normal(jax.random.fold_in(_rk, 1), (16, 512, 512), jnp.float32)
        _lenS = 512 - jax.random.randint(jax.random.fold_in(_rk, 7), (16,), 0, max(1, 512 // 4) + 1, jnp.int32)
        _lenS2 = 512 - jax.random.randint(jax.random.fold_in(_rk, 8), (16,), 0, max(1, 512 // 4) + 1, jnp.int32)
        cond_1024 = 0.00141218 + 0.997886 * jax.random.normal(jax.random.fold_in(_rk, 11), (16, 512), jnp.float32)
        return (x, cond_1024)
    x, cond_1024 = _rec_inputs()

    def _L0_cond_setup():
        import jax, jax.numpy as jnp
        import numpy as np
        B, T, C = (64, 256, 512)
        key = jax.random.key(seed)
        ks = jax.random.split(key, 17)
        s_in = 1.0 / np.sqrt(C)

        def lin(kw, kb, fan_in):
            s = 1.0 / np.sqrt(fan_in)
            W = jax.random.uniform(kw, (C, fan_in), jnp.float32, -s, s)
            b = jax.random.uniform(kb, (C,), jnp.float32, -s, s)
            return (W, b)
        Wxz, bxz = lin(ks[0], ks[1], C)
        Whz, bhz = lin(ks[2], ks[3], C)
        Wxr, bxr = lin(ks[4], ks[5], C)
        Whr, bhr = lin(ks[6], ks[7], C)
        Wxh, bxh = lin(ks[8], ks[9], C)
        Whh, bhh = lin(ks[10], ks[11], C)
        Whq, bhq = lin(ks[12], ks[13], C)
        X = jax.random.normal(ks[14], (B, T, C), jnp.float32)
        h0 = jax.random.normal(ks[15], (B, C), jnp.float32)
        return {'X': X, 'h0': h0, 'Wxz': Wxz, 'bxz': bxz, 'Whz': Whz, 'bhz': bhz, 'Wxr': Wxr, 'bxr': bxr, 'Whr': Whr, 'bhr': bhr, 'Wxh': Wxh, 'bxh': bxh, 'Whh': Whh, 'bhh': bhh, 'Whq': Whq, 'bhq': bhq}
    _L0_cond_all = _L0_cond_setup()
    _L0_cond_in = {k: v for k, v in _L0_cond_all.items() if k in ('Wxz', 'bxz', 'Whz', 'bhz', 'Wxr', 'bxr', 'Whr', 'bhr', 'Wxh', 'bxh', 'Whh', 'bhh', 'Whq', 'bhq')}
    del _L0_cond_all
    return {'x': x, 'cond_1024': cond_1024, 'L0_cond_Wxz': _L0_cond_in['Wxz'], 'L0_cond_bxz': _L0_cond_in['bxz'], 'L0_cond_Whz': _L0_cond_in['Whz'], 'L0_cond_bhz': _L0_cond_in['bhz'], 'L0_cond_Wxr': _L0_cond_in['Wxr'], 'L0_cond_bxr': _L0_cond_in['bxr'], 'L0_cond_Whr': _L0_cond_in['Whr'], 'L0_cond_bhr': _L0_cond_in['bhr'], 'L0_cond_Wxh': _L0_cond_in['Wxh'], 'L0_cond_bxh': _L0_cond_in['bxh'], 'L0_cond_Whh': _L0_cond_in['Whh'], 'L0_cond_bhh': _L0_cond_in['bhh'], 'L0_cond_Whq': _L0_cond_in['Whq'], 'L0_cond_bhq': _L0_cond_in['bhq']}

def reference(x, cond_1024, L0_cond_Wxz, L0_cond_bxz, L0_cond_Whz, L0_cond_bhz, L0_cond_Wxr, L0_cond_bxr, L0_cond_Whr, L0_cond_bhr, L0_cond_Wxh, L0_cond_bxh, L0_cond_Whh, L0_cond_bhh, L0_cond_Whq, L0_cond_bhq):
    import jax
    import jax.numpy as jnp

    def _L0_cond_ref(X, h0, Wxz, bxz, Whz, bhz, Wxr, bxr, Whr, bhr, Wxh, bxh, Whh, bhh, Whq, bhq):
        import jax, jax.numpy as jnp
        import numpy as np
        B, T, C = (64, 256, 512)
        Xz = jnp.einsum('btc,hc->tbh', X, Wxz) + bxz
        Xr = jnp.einsum('btc,hc->tbh', X, Wxr) + bxr
        Xh = jnp.einsum('btc,hc->tbh', X, Wxh) + bxh

        def step(H, xs):
            xz, xr, xh = xs
            Z = jax.nn.sigmoid(xz + H @ Whz.T + bhz)
            R = jax.nn.sigmoid(xr + H @ Whr.T + bhr)
            H_tilda = jnp.tanh(xh + R * H @ Whh.T + bhh)
            H_new = Z * H + (1.0 - Z) * H_tilda
            Y = H_new @ Whq.T + bhq
            return (H_new, Y)
        _, Ys = jax.lax.scan(step, h0, (Xz, Xr, Xh))
        return jnp.transpose(Ys, (1, 0, 2))
    x = x + _L0_cond_ref(x, cond_1024, L0_cond_Wxz, L0_cond_bxz, L0_cond_Whz, L0_cond_bhz, L0_cond_Wxr, L0_cond_bxr, L0_cond_Whr, L0_cond_bhr, L0_cond_Wxh, L0_cond_bxh, L0_cond_Whh, L0_cond_bhh, L0_cond_Whq, L0_cond_bhq)
    return x

_drawn_inputs = setup_inputs


def setup_inputs(seed=0):
    import zlib

    import numpy as np

    out = dict(_drawn_inputs(seed))
    spreads = {}
    factors = {'cond_1024': 3.353,
     'L0_cond_bxz': 22.801,
     'L0_cond_Whz': 4.098,
     'L0_cond_bhz': 24.378,
     'L0_cond_Wxr': 8.0,
     'L0_cond_bxr': 200.0,
     'L0_cond_Whr': 8.0,
     'L0_cond_bhr': 200.0,
     'L0_cond_bxh': 4.701,
     'L0_cond_bhh': 4.614}
    for name, (base, spread) in spreads.items():
        noise = np.random.default_rng([zlib.crc32(name.encode()), seed]).standard_normal(out[name].shape)
        drawn = base * np.exp(spread * noise) if base else spread * noise
        out[name] = jnp.asarray(drawn.astype(out[name].dtype))
    for name, factor in factors.items():
        out[name] = (out[name] * factor).astype(out[name].dtype)
    return out
```

```python
from contextlib import ExitStack

import concourse.bass as bass
from concourse import mybir

F32 = mybir.dt.float32
BF16 = mybir.dt.bfloat16
ALU = mybir.AluOpType
ACT = mybir.ActivationFunctionType

P = 128
G = 4
Q = 32
BLOCK_PAIRS = 8
HALF = BLOCK_PAIRS // 2
R, Z, H = range(3)

X_UNITS = [(g, u) for g in (R, Z, H) for u in range(G + 1)]
Y_UNITS = [("y", u) for u in range(G + 1)]


def gru(nc, x, h0, w_x, b_x, w_h, b_h, w_q, b_q, out):
    batch, steps, chans = x.shape
    assert chans == G * P and 2 * batch == Q
    pairs = steps // 2
    blocks = pairs // BLOCK_PAIRS
    fill = Y_UNITS + X_UNITS
    gaps = [[fill[0:2], fill[2:10]], [fill[10:12], fill[12:20]]]

    with ExitStack() as ctx:
        def sb(name, shape, dt=F32):
            return ctx.enter_context(nc.sbuf_tensor(name, shape, dt))

        def sem(name):
            return ctx.enter_context(nc.semaphore(name))

        mats = [*w_x, *w_h, w_q]
        w_raw = sb("w_raw", [P, len(mats), G, chans])
        w_mov = sb("w_mov", [P, len(mats), G, chans])
        ident = sb("ident", [P, P])
        bias_raw = sb("bias_raw", [P, 4, chans])
        bias_rest = sb("bias_rest", [P, 4, chans])
        bias_part = sb("bias_part", [P, 3, 4, chans], BF16)
        bias_mov = sb("bias_mov", [P, 4, chans], BF16)
        ones = sb("ones", [P, Q], BF16)
        x_in = sb("x_in", [P, BLOCK_PAIRS, P])
        y_out = sb("y_out", [P, BLOCK_PAIRS, P])
        x_t = sb("x_t", [P, 4, G, Q])
        h0_in = sb("h0_in", [P, P])
        state = sb("state", [P, 16 + G * Q])
        reset_state = sb("reset_state", [P, 16 + G * Q])
        state_pair = sb("state_pair", [P, 2, G, 2, 16])
        pre_t = [sb(f"pre_t{g}", [P, G, 2, 16]) for g in range(3)]
        r_gate = sb("r_gate", [P, G, 16])
        z_gate = sb("z_gate", [P, G, 16])
        z_not = sb("z_not", [P, G, 16])
        cand = sb("cand", [P, G, 16])
        kept = sb("kept", [P, G, 16])
        fresh = sb("fresh", [P, G, 16])

        pre = [[ctx.enter_context(nc.psum_tensor(f"pre{g}{n}", [P, 512], F32)) for n in range(2)]
               for g in range(3)]
        y_ps = ctx.enter_context(nc.psum_tensor("y_ps", [P, 512], F32))
        spare = ctx.enter_context(nc.psum_tensor("spare", [P, 512], F32))
        banks = [pre[0][0], pre[0][1], pre[1][0], pre[1][1], pre[2][0], pre[2][1], y_ps, spare]

        zeroed = sem("zeroed")
        ident_ready = sem("ident_ready")
        w_loaded = [sem(f"w_loaded{m}") for m in range(len(mats))]
        bias_loaded = sem("bias_loaded")
        bias_step = sem("bias_step")
        bias_ready = sem("bias_ready")
        h0_loaded = sem("h0_loaded")
        w_turned = sem("w_turned")
        w_copied = [sem("w_copied_dve"), sem("w_copied_act")]
        x_loaded = [sem("x_loaded0"), sem("x_loaded1")]
        x_turned = sem("x_turned")
        pre_done = [sem("r_pre_done"), sem("z_pre_done"), sem("h_pre_done")]
        pre_turned = [sem("r_pre_turned"), sem("z_pre_turned"), sem("h_pre_turned")]
        r_ready = sem("r_ready")
        z_ready = sem("z_ready")
        z_not_ready = sem("z_not_ready")
        cand_ready = sem("cand_ready")
        reset_ready = sem("reset_ready")
        kept_ready = sem("kept_ready")
        fresh_ready = sem("fresh_ready")
        state_ready = sem("state_ready")
        pair_ready = sem("pair_ready")
        y_done = sem("y_done")
        y_added = sem("y_added")
        stored = [sem("stored0"), sem("stored1")]

        block = ctx.enter_context(nc.Block())

        def cols(t):
            return t[:, 16:16 + G * Q].rearrange("p (m c) -> p m c", m=G)[:, :, 0:16]

        def window(t, m, s):
            a = Q * m + 16 - 16 * s
            return t[:, a:a + Q]

        def by_block(t):
            return t.rearrange("p (i m) -> p m i", m=G)

        def w_copy(n):
            to, of = w_mov[:, n // G, n % G, :], banks[n % 8][:]
            if n // G < 6:
                to = to.rearrange("p (j m i) -> p j m i", j=G, m=G)
                of = of.rearrange("p (j i m) -> p j m i", j=G, m=G)
            return to, of

        x_v = x.rearrange("b (h q s) (j n) -> h s j b q n", q=HALF, s=2, j=G)
        out_v = out.rearrange("b (h q s) (j n) -> h s j b q n", q=HALF, s=2, j=G)

        @block.sync
        def _(sp):
            def load(half, i):
                for s in range(2):
                    for j in range(G):
                        p = Q * j + 16 * s
                        sp.dma_start(x_in[p:p + 16, half * HALF:(half + 1) * HALF, :],
                                     x_v[2 * i + half, s, j]).then_inc(x_loaded[half], 16)

            def store(half, i):
                for s in range(2):
                    for j in range(G):
                        p = Q * j + 16 * s
                        sp.dma_start(out_v[2 * i + half, s, j],
                                     y_out[p:p + 16, half * HALF:(half + 1) * HALF, :]
                                     ).then_inc(stored[half], 16)

            def turn(i, last):
                for half in range(2):
                    sp.wait_ge(y_added, i * BLOCK_PAIRS + (half + 1) * HALF)
                    store(half, i)
                    if not last:
                        load(half, i + 1)

            sp.wait_ge(zeroed, 1)
            for j in range(G):
                sp.dma_start(h0_in[Q * j:Q * j + 16, :], h0[:, P * j:P * (j + 1)]).then_inc(h0_loaded, 16)
            for a in range(3):
                for g in range(4):
                    if g < 3:
                        sp.dma_start(bias_raw[Q * a:Q * a + 1, g, :], b_x[g].rearrange("(a n) -> a n", a=1)
                                     ).then_inc(bias_loaded, 16)
                    sp.dma_start(bias_raw[Q * a + 1:Q * a + 2, g, :],
                                 (b_h[g] if g < 3 else b_q).rearrange("(a n) -> a n", a=1)
                                 ).then_inc(bias_loaded, 16)
            load(0, 0)
            load(1, 0)
            with sp.Fori(0, blocks - 1) as i:
                turn(i, last=False)
            turn(blocks - 1, last=True)
            for half in range(2):
                sp.wait_ge(stored[half], blocks * 8 * 16)

        @block.gpsimd
        def _(pool):
            nc.gpsimd.memset(h0_in[:], 0.0)
            nc.gpsimd.memset(bias_raw[:], 0.0).then_inc(zeroed, 1)
            nc.gpsimd.memset(ident[:], 0.0).then_inc(ident_ready, 1)
            pool.wait_ge(ident_ready, 1)
            nc.gpsimd.affine_select(out=ident[:], in_=ident[:], compare_op=ALU.not_equal, fill=1.0,
                                    base=0, pattern=[[-1, P]], channel_multiplier=1
                                    ).then_inc(ident_ready, 1)

        @block.tensor
        def _(pe):
            def unit(what, u, k, s_buf):
                if what == "y":
                    dst, bias, mat, stat = y_ps, 3, 6, state_pair[:, s_buf]
                else:
                    dst, bias, mat, stat = pre[what][k % 2], what, what, x_t[:, k % 4]
                for j in range(G):
                    o = dst[Q * j:Q * (j + 1), 0:P]
                    if u == 0:
                        mm = nc.tensor.matmul(o, ones[:], bias_mov[:, bias, P * j:P * (j + 1)],
                                              start=True, stop=False, skip_group_check=True)
                    else:
                        m = u - 1
                        st = stat[:, m].rearrange("p s b -> p (s b)") if what == "y" else stat[:, m, :]
                        mm = nc.tensor.matmul(o, st, w_mov[:, mat, m, P * j:P * (j + 1)],
                                              start=False, stop=(m == G - 1), skip_group_check=True)
                return mm

            def recur(g, src, k, s):
                for m in range(G):
                    for j in range(G):
                        mm = nc.tensor.matmul(pre[g][k % 2][Q * j:Q * (j + 1), 0:P], window(src, m, s),
                                              w_mov[:, 3 + g, m, P * j:P * (j + 1)], start=False,
                                              stop=(m == G - 1), skip_group_check=True)
                mm.then_inc(pre_done[g], 1)

            def run(units, i, k, first, last):
                for what, u in units:
                    if what == "y":
                        if first and k == 0:
                            continue
                        if u == 0:
                            pe.wait_ge(pair_ready, i * 2 * BLOCK_PAIRS + 2 * k)
                            if not (first and k == 1):
                                pe.wait_ge(y_added, i * BLOCK_PAIRS + k - 1)
                        mm = unit(what, u, k - 1, (k - 1) % 2)
                        if u == G:
                            mm.then_inc(y_done, 1)
                    else:
                        if last and k == BLOCK_PAIRS - 1:
                            continue
                        if what == R and u == 1:
                            pe.wait_ge(x_turned, i * BLOCK_PAIRS + k + 2)
                        unit(what, u, k + 1, None)

            def turn(i, first, last):
                for k in range(BLOCK_PAIRS):
                    for s in range(2):
                        t = i * 2 * BLOCK_PAIRS + 2 * k + s
                        pe.wait_ge(state_ready, t + 1)
                        recur(R, state, k, s)
                        recur(Z, state, k, s)
                        run(gaps[s][0], i, k, first, last)
                        pe.wait_ge(reset_ready, t + 1)
                        recur(H, reset_state, k, s)
                        run(gaps[s][1], i, k, first, last)

            pe.wait_ge(ident_ready, 2)
            for n in range(len(mats) * G):
                mat, m = divmod(n, G)
                if m == 0:
                    pe.wait_ge(w_loaded[mat], 16)
                if n >= 8:
                    pe.wait_ge(w_copied[n % 2], (n - 8) // 2 + 1)
                for j in range(G):
                    w = w_raw[:, mat, j, :].rearrange("p (c m) -> p m c", m=G)[:, m, :]
                    mm = nc.tensor.transpose(banks[n % 8][:, P * j:P * (j + 1)], w, ident[:])
                mm.then_inc(w_turned, 1)
            for e in range(2):
                pe.wait_ge(w_copied[e], len(mats) * G // 2)
            pe.wait_ge(bias_ready, 1 + 3 * 4)
            pe.wait_ge(x_turned, 1)
            for what, u in X_UNITS:
                unit(what, u, 0, None)
            turn(0, first=True, last=False)
            with pe.Fori(1, blocks - 1) as i:
                turn(i, first=False, last=False)
            turn(blocks - 1, first=False, last=True)
            pe.wait_ge(pair_ready, 2 * pairs)
            pe.wait_ge(y_added, pairs - 1)
            for what, u in Y_UNITS:
                mm = unit(what, u, BLOCK_PAIRS - 1, (BLOCK_PAIRS - 1) % 2)
            mm.then_inc(y_done, 1)

        @block.scalar
        def _(act):
            for m, w in enumerate(mats):
                act.dma_start(w_raw[:, m], w.rearrange("(j n) c -> n j c", j=G)).then_inc(w_loaded[m], 16)
            for n in range(1, len(mats) * G, 2):
                act.wait_ge(w_turned, n + 1)
                nc.scalar.copy(*w_copy(n)).then_inc(w_copied[1], 1)

            def turn(i, first):
                for k in range(BLOCK_PAIRS):
                    for s in range(2):
                        t = i * 2 * BLOCK_PAIRS + 2 * k + s
                        act.wait_ge(pre_turned[R], t + 1)
                        nc.scalar.activation(r_gate[:], pre_t[R][:, :, s, :], ACT.Sigmoid).then_inc(r_ready, 1)
                        act.wait_ge(pre_turned[Z], t + 1)
                        nc.scalar.activation(z_gate[:], pre_t[Z][:, :, s, :], ACT.Sigmoid).then_inc(z_ready, 1)
                        nc.scalar.activation(z_not[:], pre_t[Z][:, :, s, :], ACT.Sigmoid, scale=-1.0
                                             ).then_inc(z_not_ready, 1)
                        act.wait_ge(pre_turned[H], t + 1)
                        nc.scalar.activation(cand[:], pre_t[H][:, :, s, :], ACT.Tanh).then_inc(cand_ready, 1)
                        if s == 0 and not (first and k < 2):
                            act.wait_ge(y_done, i * BLOCK_PAIRS + k - 1)
                        act.wait_ge(state_ready, t + 2)
                        nc.scalar.copy(state_pair[:, k % 2, :, s, :], cols(state)).then_inc(pair_ready, 1)

            turn(0, first=True)
            with act.Fori(1, blocks) as i:
                turn(i, first=False)

        @block.vector
        def _(dve):
            nc.vector.memset(state[:], 0.0)
            nc.vector.memset(reset_state[:], 0.0)
            nc.vector.memset(ones[:], 1.0)
            nc.vector.memset(bias_mov[:], 0.0).then_inc(bias_ready, 1)
            dve.wait_ge(bias_loaded, 21 * 16)
            nc.vector.tensor_copy(bias_part[:, 0], bias_raw[:]).then_inc(bias_step, 1)
            dve.wait_ge(bias_step, 1)
            nc.vector.tensor_tensor(bias_rest[:], bias_raw[:], bias_part[:, 0], ALU.subtract).then_inc(bias_step, 1)
            dve.wait_ge(bias_step, 2)
            nc.vector.tensor_copy(bias_part[:, 1], bias_rest[:]).then_inc(bias_step, 1)
            dve.wait_ge(bias_step, 3)
            nc.vector.tensor_tensor(bias_part[:, 2], bias_rest[:], bias_part[:, 1], ALU.subtract).then_inc(bias_step, 1)
            dve.wait_ge(bias_step, 4)
            dve.wait_ge(bias_ready, 1)
            for a in range(3):
                rows = slice(Q * a, Q * a + 2)
                for g in range(3):
                    nc.vector.tensor_copy(
                        bias_mov[rows, g].rearrange("p (j m i) -> p j m i", j=G, m=G),
                        bias_part[rows, a, g].rearrange("p (j i m) -> p j m i", j=G, m=G)
                    ).then_inc(bias_ready, 1)
                nc.vector.tensor_copy(bias_mov[rows, 3], bias_part[rows, a, 3]).then_inc(bias_ready, 1)
            for n in range(0, len(mats) * G, 2):
                dve.wait_ge(w_turned, n + 1)
                nc.vector.tensor_copy(*w_copy(n)).then_inc(w_copied[0], 1)
            dve.wait_ge(h0_loaded, G * 16)
            nc.vector.transpose(state[:, 16:16 + G * Q].rearrange("p (m c) -> p m c", m=G), by_block(h0_in[:])).then_inc(state_ready, 1)

            def x_turn(k):
                nc.vector.transpose(x_t[:, k % 4], by_block(x_in[:, k, :])
                                    ).then_inc(x_turned, 1)

            def pre_turn(g, k):
                nc.vector.transpose(pre_t[g][:].rearrange("p m s b -> p (m s b)"), pre[g][k % 2][:, 0:P]
                                    ).then_inc(pre_turned[g], 1)

            def y_add(n, k, need_store):
                dve.wait_ge(y_done, n + 1)
                if need_store is not None:
                    dve.wait_ge(stored[k // HALF], need_store)
                nc.vector.tensor_tensor(y_out[:, k, :], y_ps[:, 0:P], x_in[:, k, :], ALU.add
                                        ).then_inc(y_added, 1)

            def turn(i, first, last):
                for k in range(BLOCK_PAIRS):
                    for s in range(2):
                        t = i * 2 * BLOCK_PAIRS + 2 * k + s
                        dve.wait_ge(pre_done[R], t + 1)
                        pre_turn(R, k)
                        if s == 0 and not (last and k >= BLOCK_PAIRS - 2):
                            ahead = k + 2
                            if ahead % HALF == 0:
                                dve.wait_ge(x_loaded[(ahead // HALF) % 2],
                                            (i + ahead // BLOCK_PAIRS + 1) * 8 * 16)
                            x_turn(ahead % BLOCK_PAIRS)
                        dve.wait_ge(r_ready, t + 1)
                        dve.wait_ge(state_ready, t + 1)
                        nc.vector.tensor_tensor(cols(reset_state), r_gate[:], cols(state), ALU.mult
                                                ).then_inc(reset_ready, 1)
                        dve.wait_ge(pre_done[Z], t + 1)
                        pre_turn(Z, k)
                        dve.wait_ge(z_ready, t + 1)
                        nc.vector.tensor_tensor(kept[:], z_gate[:], cols(state), ALU.mult
                                                ).then_inc(kept_ready, 1)
                        if s == 1 and not (first and k == 0):
                            n = i * BLOCK_PAIRS + k - 1
                            need = i * 8 * 16 if not first and k > 0 and (k - 1) % HALF == 0 else None
                            y_add(n, (k - 1) % BLOCK_PAIRS, need)
                        dve.wait_ge(pre_done[H], t + 1)
                        pre_turn(H, k)
                        dve.wait_ge(cand_ready, t + 1)
                        dve.wait_ge(z_not_ready, t + 1)
                        nc.vector.tensor_tensor(fresh[:], z_not[:], cand[:], ALU.mult).then_inc(fresh_ready, 1)
                        dve.wait_ge(fresh_ready, t + 1)
                        dve.wait_ge(kept_ready, t + 1)
                        if not (first and k == 0 and s == 0):
                            dve.wait_ge(pair_ready, t)
                        nc.vector.tensor_tensor(cols(state), fresh[:], kept[:], ALU.add).then_inc(state_ready, 1)

            dve.wait_ge(x_loaded[0], 8 * 16)
            x_turn(0)
            x_turn(1)
            turn(0, first=True, last=False)
            with dve.Fori(1, blocks - 1) as i:
                turn(i, first=False, last=False)
            turn(blocks - 1, first=False, last=True)
            y_add(pairs - 1, BLOCK_PAIRS - 1, None)


_W = "L0_cond_"
_INS = ["x", "cond_1024"] + [_W + n for n in ("Wxr", "Wxz", "Wxh", "bxr", "bxz", "bxh", "Whr", "Whz", "Whh",
                                              "bhr", "bhz", "bhh", "Whq", "bhq")]


def kernel(**inputs):
    import numpy as _np
    import concourse.bacc as _bacc
    from concourse import mybir as _mybir
    from concourse.bass_utils import run_bass_kernel_spmd as _run

    nc = _bacc.Bacc("TRN2", target_bir_lowering=False, num_devices=1)
    arrays, a = {}, {}
    for name in _INS:
        v = _np.ascontiguousarray(inputs[name])
        arrays[f"in_{name}"] = v
        a[name] = nc.dram_tensor(f"in_{name}", v.shape, _mybir.dt.from_np(v.dtype), kind="ExternalInput").ap()
    shape = inputs["x"].shape
    out = nc.dram_tensor("out", shape, _mybir.dt.float32, kind="ExternalOutput").ap()

    def of(kind):
        return [a[f"{_W}{kind}{g}"] for g in "rzh"]

    gru(nc, a["x"], a["cond_1024"], of("Wx"), of("bx"), of("Wh"), of("bh"), a[_W + "Whq"], a[_W + "bhq"], out)
    r = _run(nc, [arrays], core_ids=[0])
    return r.results[0]["out"]
```

```python
from contextlib import ExitStack

import concourse.bass as bass
from concourse import mybir

F32 = mybir.dt.float32
F32R = mybir.dt.float32r
BF16 = mybir.dt.bfloat16
ALU = mybir.AluOpType
ACT = mybir.ActivationFunctionType

P = 128
G = 4
Q = 32
B = 16
TS = P // B
UNROLL = 2
PARTS = [(0, 2), (2, 4)]
NP = len(PARTS)
HI, LO = range(2)
R, Z, H = range(3)
RT, ZT, HT, Y, T = range(3, 8)
JOB_BANK = {R: 0, Z: 1, H: 2, RT: 3, ZT: 4, HT: 0, Y: 1, T: 3}

PROJECT = ([(HI, w, m) for m in range(G) for w in (HI, LO)] + [(LO, HI, m) for m in range(G)])
UNITS = {job: PROJECT for job in (R, Z, H)} | {job: list(range(G)) for job in (RT, ZT, HT, T)}
UNITS[Y] = ["bias"] + PROJECT
BACKGROUND = [
    [(R, 0, 7)],
    [(R, 7, 12), (Z, 0, 2)],
    [(Z, 2, 9)],
    [(RT, 0, 4), (Z, 9, 12), (H, 0, 2)],
    [(H, 2, 9)],
    [(ZT, 0, 4), (H, 9, 12), (Y, 0, 2)],
    [(Y, 2, 9)],
    [(HT, 0, 4), (Y, 9, 13), (T, 0, 4)],
]
SCALAR_JOBS = {0: ["x_hi", HT], 1: ["states_hi"], 3: ["residual"], 4: [RT], 6: [ZT]}
VECTOR_JOBS = {0: [Y], 1: ["x_lo"], 2: [R], 3: ["states_lo"], 4: [Z], 6: [H]}


def gru(nc, x, h0, w_x, b_x, w_h, b_h, w_q, b_q, out):
    batch, steps, chans = x.shape
    assert batch == B and chans == G * P
    tiles = steps // TS
    turns = tiles // UNROLL

    with ExitStack() as ctx:
        def sb(name, shape, dt=F32):
            return ctx.enter_context(nc.sbuf_tensor(name, shape, dt))

        def bank(name):
            return ctx.enter_context(nc.psum_tensor(name, [P, 512], F32))

        def sem(name):
            return ctx.enter_context(nc.semaphore(name))

        mats = [*w_x, w_q, *w_h]
        n_split = 4
        w_raw = sb("w_raw", [P, len(mats), G, chans])
        w_split = [sb(f"w_split{a}", [P, n_split, G, chans], F32R) for a in (HI, LO)]
        w_gate = sb("w_gate", [P, 3, G, chans])
        ident = sb("ident", [P, P])
        bias_raw = sb("bias_raw", [P, 3, chans])
        bias_gate = sb("bias_gate", [P, 3, chans])
        bq_raw = sb("bq_raw", [P, chans])
        bq_rest = sb("bq_rest", [P, chans])
        bq_part = sb("bq_part", [P, 3, chans], BF16)
        bq_mov = sb("bq_mov", [P, chans], BF16)
        ones = sb("ones", [P, P], BF16)
        x_in = sb("x_in", [P, 2, chans])
        x_rows = sb("x_rows", [P, 3, chans])
        y_out = sb("y_out", [P, 2, chans])
        x_part = [sb(f"x_part{a}", [P, G, P], F32R) for a in (HI, LO)]
        states = sb("states", [P, 2, G, B, TS])
        states_part = [sb(f"states_part{a}", [P, G, P], F32R) for a in (HI, LO)]
        x_gate = sb("x_gate", [P, 2, 3, TS, G, B])
        h0_in = sb("h0_in", [P, P])
        state = sb("state", [P, G, B])
        reset_state = sb("reset_state", [P, G, B])
        pre_t = [sb(f"pre_t{g}", [P, G, Q]) for g in range(3)]
        pre_sum = [sb(f"pre_sum{g}", [P, G, B]) for g in range(3)]
        r_gate = sb("r_gate", [P, G, B])
        z_gate = sb("z_gate", [P, G, B])
        z_not = sb("z_not", [P, G, B])
        cand = sb("cand", [P, G, B])
        kept = sb("kept", [P, G, B])
        fresh = sb("fresh", [P, G, B])

        pre = [bank(f"pre{g}") for g in range(3)]
        job_bank = [bank(f"job{n}") for n in range(5)]
        banks = [*pre, *job_bank]

        zeroed = sem("zeroed")
        ident_ready = sem("ident_ready")
        w_loaded = [sem(f"w_loaded{m}") for m in range(len(mats))]
        bias_loaded = sem("bias_loaded")
        bias_ready = sem("bias_ready")
        bq_loaded = sem("bq_loaded")
        bq_step = sem("bq_step")
        bq_ready = sem("bq_ready")
        h0_loaded = sem("h0_loaded")
        h0_turned = sem("h0_turned")
        w_turned = sem("w_turned")
        w_hi_ready = sem("w_hi_ready")
        bank_free = [sem(f"bank_free{n}") for n in range(8)]
        x_loaded = [sem("x_loaded0"), sem("x_loaded1")]
        names = ("xr", "xz", "xh", "xr_t", "xz_t", "xh_t", "y", "x_t")
        job_done = [sem(f"done_{n}") for n in names]
        job_copied = [sem(f"copied_{n}") for n in names]
        x_hi_ready = sem("x_hi_ready")
        states_hi_ready = sem("states_hi_ready")
        states_lo_ready = sem("states_lo_ready")
        residual_put = sem("residual_put")
        pre_done = [sem("r_pre_done"), sem("z_pre_done"), sem("h_pre_done")]
        pre_turned = [sem("r_pre_turned"), sem("z_pre_turned"), sem("h_pre_turned")]
        pre_summed = [sem("r_pre_summed"), sem("z_pre_summed"), sem("h_pre_summed")]
        r_ready = sem("r_ready")
        z_ready = sem("z_ready")
        z_not_ready = sem("z_not_ready")
        cand_ready = sem("cand_ready")
        reset_ready = sem("reset_ready")
        kept_ready = sem("kept_ready")
        fresh_ready = sem("fresh_ready")
        state_ready = sem("state_ready")
        state_kept = sem("state_kept")
        stored = [sem("stored0"), sem("stored1")]

        block = ctx.enter_context(nc.Block())

        def by_block(t):
            if t.shape[-1] == P:
                return t.rearrange("p (i m) -> p m i", m=G)
            return t.rearrange("p (j i m) -> p j m i", j=G, m=G)

        def turnable(t, m):
            return t.rearrange("p (c m) -> p m c", m=G)[:, m, :]

        x_v = x.rearrange("b (n t) c -> n b t c", t=TS)
        out_v = out.rearrange("b (n t) c -> n b t c", t=TS)

        def tile_loop(eng, tile):
            for par in range(UNROLL):
                tile(0, par, first=True, last=False)
            with eng.Fori(1, turns - 1) as i:
                for par in range(UNROLL):
                    tile(i, par, first=False, last=False)
            for par in range(UNROLL):
                tile(turns - 1, par, first=False, last=True)

        @block.sync
        def _(sp):
            def load(n, par):
                sp.dma_start(x_in[:, par, :], x_v[n]).then_inc(x_loaded[par], 16)

            def store(n, par):
                sp.dma_start(out_v[n], y_out[:, par, :]).then_inc(stored[par], 16)

            def tile(i, par, first, last):
                n = i * UNROLL + par
                if not first:
                    sp.wait_ge(job_copied[Y], n - 1)
                    store(n - 2, par)
                if not last:
                    sp.wait_ge(residual_put, n + 1)
                    load(n + 2, par)

            sp.wait_ge(zeroed, 1)
            for par in range(2):
                load(par, par)
            for j in range(G):
                sp.dma_start(h0_in[Q * j:Q * j + B, :], h0[:, P * j:P * (j + 1)]).then_inc(h0_loaded, 16)
            for a in range(3):
                sp.dma_start(bq_raw[Q * a:Q * a + 1, :], b_q.rearrange("(a n) -> a n", a=1)
                             ).then_inc(bq_loaded, 16)
            for a, b in enumerate((b_x, b_h)):
                for g in range(3):
                    sp.dma_start((bias_gate if a == 0 else bias_raw)[:, g, :],
                                 b[g].rearrange("(a n) -> a n", a=1).to_broadcast([P, chans])
                                 ).then_inc(bias_loaded, 16)
            tile_loop(sp, tile)
            for par in range(2):
                sp.wait_ge(job_copied[Y], tiles - 1 + par)
                store(tiles - 2 + par, par)
            for par in range(2):
                sp.wait_ge(stored[par], tiles // 2 * 16)

        @block.gpsimd
        def _(pool):
            nc.gpsimd.memset(h0_in[:], 0.0)
            nc.gpsimd.memset(bq_raw[:], 0.0).then_inc(zeroed, 1)
            nc.gpsimd.memset(ident[:], 0.0).then_inc(ident_ready, 1)
            pool.wait_ge(ident_ready, 1)
            nc.gpsimd.affine_select(out=ident[:], in_=ident[:], compare_op=ALU.not_equal, fill=1.0,
                                    base=0, pattern=[[-1, P]], channel_multiplier=1
                                    ).then_inc(ident_ready, 1)

        @block.tensor
        def _(pe):
            def unit(job, k, par):
                to = job_bank[JOB_BANK[job]]
                u = UNITS[job][k]
                if job == T:
                    mm = nc.tensor.transpose(to[:, P * u:P * (u + 1)], turnable(x_in[:, par, :], u), ident[:])
                elif job in (RT, ZT, HT):
                    mm = nc.tensor.transpose(to[:, P * u:P * (u + 1)], turnable(x_rows[:, job - RT, :], u),
                                             ident[:])
                elif u == "bias":
                    mm = nc.tensor.matmul(to[:], ones[:], bq_mov[:], start=True, stop=False)
                else:
                    a, w, m = u
                    of = states_part if job == Y else x_part
                    mat = 3 if job == Y else job
                    mm = nc.tensor.matmul(to[:], of[a][:, m, :], w_split[w][:, mat, m, :],
                                          start=(k == 0), stop=(k == len(UNITS[job]) - 1))
                if k == len(UNITS[job]) - 1:
                    mm.then_inc(job_done[job], 1)

            def wait_for(job, k, n, i, par, first, last):
                if job in (R, Z, H) and k == 0:
                    pe.wait_ge(x_hi_ready, n + 2)
                    if job == R:
                        pe.wait_ge(job_copied[HT], n + 1)
                    elif job == H:
                        pe.wait_ge(job_copied[H], n + 1)
                    elif not first:
                        pe.wait_ge(job_copied[Y], n - 1)
                elif job in (R, Z, H) and UNITS[job][k] == (LO, HI, 0):
                    pe.wait_ge(job_copied[T], n + 2)
                elif job in (RT, ZT, HT) and k == 0:
                    pe.wait_ge(job_copied[job - RT], n + 2)
                    if job == RT:
                        pe.wait_ge(job_copied[T], n + 2)
                    elif job == ZT:
                        pe.wait_ge(job_copied[ZT], n + 1)
                elif job == Y and k == 0:
                    if last and par == 1:
                        pe.wait_ge(job_copied[Y], n - 1)
                    else:
                        pe.wait_ge(job_copied[Z], n + 2)
                elif job == Y and UNITS[job][k] == (HI, HI, 0):
                    pe.wait_ge(states_hi_ready, n)
                elif job == Y and UNITS[job][k] == (LO, HI, 0):
                    pe.wait_ge(states_lo_ready, n)
                elif job == T and k == 0:
                    pe.wait_ge(x_loaded[par], (i + 2) * 16)
                    pe.wait_ge(job_copied[RT], n + 2)

            def recur(g, src, ready, n_ready):
                for m in range(G):
                    for h, (a, _) in enumerate(PARTS):
                        if m == a:
                            pe.wait_ge(ready, n_ready + h)
                    for j in range(G):
                        mm = nc.tensor.matmul(pre[g][Q * j:Q * j + B, 0:P], src[:, m, :],
                                              w_gate[:, g, m, P * j:P * (j + 1)], start=(m == 0),
                                              stop=(m == G - 1))
                mm.then_inc(pre_done[g], 1)

            def tile(i, par, first, last):
                n = i * UNROLL + par
                for step in range(TS):
                    t = n * TS + step
                    recur(R, state, state_ready, t * NP + 1)
                    recur(Z, state, state_ready, t * NP + 1)
                    recur(H, reset_state, reset_ready, t * NP + 1)
                    for job, a, b in BACKGROUND[step]:
                        if job == Y and first and par == 0:
                            continue
                        if job == T and last or job in (R, Z, H, RT, ZT, HT) and last and par == 1:
                            continue
                        for k in range(a, b):
                            wait_for(job, k, n, i, par, first, last)
                            unit(job, k, par)

            pe.wait_ge(ident_ready, 2)
            for n in range(len(mats) * G):
                mat, m = divmod(n, G)
                if m == 0:
                    pe.wait_ge(w_loaded[mat], 16)
                if n >= 8:
                    pe.wait_ge(bank_free[n % 8], n // 8)
                for j in range(G):
                    mm = nc.tensor.transpose(banks[n % 8][:, P * j:P * (j + 1)],
                                             turnable(w_raw[:, mat, j, :], m), ident[:])
                mm.then_inc(w_turned, 1)
            for n in range(8):
                pe.wait_ge(bank_free[n], (len(mats) * G - 1 - n) // 8 + 1)
            pe.wait_ge(bq_ready, 4)
            for par in range(2):
                pe.wait_ge(x_loaded[par], 16)
                if par == 1:
                    pe.wait_ge(job_copied[RT], 1)
                for k in range(G):
                    unit(T, k, par)
                if par == 0:
                    pe.wait_ge(x_hi_ready, 1)
                    pe.wait_ge(job_copied[T], 1)
                    for g in (R, Z, H):
                        for k in range(len(PROJECT)):
                            unit(g, k, 0)
                    for g in (R, Z, H):
                        pe.wait_ge(job_copied[g], 1)
                        for k in range(G):
                            unit(RT + g, k, 0)
            tile_loop(pe, tile)
            pe.wait_ge(job_copied[Y], tiles - 1)
            pe.wait_ge(states_hi_ready, tiles)
            pe.wait_ge(states_lo_ready, tiles)
            for k in range(len(UNITS[Y])):
                unit(Y, k, 0)

        @block.scalar
        def _(act):
            for m, w in enumerate(mats):
                act.dma_start(w_raw[:, m], w.rearrange("(j n) c -> n j c", j=G)).then_inc(w_loaded[m], 16)
            for n in range(len(mats) * G):
                mat, m = divmod(n, G)
                if mat < n_split:
                    act.wait_ge(w_turned, n + 1)
                    nc.scalar.copy(w_split[HI][:, mat, m, :], banks[n % 8][:]).then_inc(w_hi_ready, 1)
                elif n % 2:
                    act.wait_ge(w_turned, n + 1)
                    nc.scalar.copy(w_gate[:, mat - n_split, m, :].rearrange("p (j m i) -> p j m i", j=G, m=G),
                                   by_block(banks[n % 8][:])).then_inc(bank_free[n % 8], 1)

            def copy_x_hi(n):
                act.wait_ge(job_done[T], n + 1)
                nc.scalar.copy(x_part[HI][:].rearrange("p m c -> p (m c)"), job_bank[JOB_BANK[T]][:]
                               ).then_inc(x_hi_ready, 1)

            def copy_x_gate(job, n, par):
                act.wait_ge(job_done[job], n + 1)
                nc.scalar.copy(x_gate[:, par, job - RT],
                               job_bank[JOB_BANK[job]][:].rearrange("p (m b t) -> p t m b", m=G, b=B)
                               ).then_inc(job_copied[job], 1)

            def copy_states_hi(n, par):
                act.wait_ge(state_kept, n * TS + TS)
                nc.scalar.copy(states_part[HI][:].rearrange("p m c -> p (m c)"),
                               states[:, par].rearrange("p m b t -> p (m b t)")).then_inc(states_hi_ready, 1)

            def put_residual(i, n, par, first):
                if not first:
                    act.wait_ge(stored[par], i * 16)
                nc.scalar.copy(y_out[:, par, :], x_in[:, par, :]).then_inc(residual_put, 1)

            def tile(i, par, first, last):
                n = i * UNROLL + par
                for step in range(TS):
                    t = n * TS + step
                    for job in SCALAR_JOBS.get(step, []):
                        if job == "x_hi" and not (first and par == 0) and not (last and par == 1):
                            copy_x_hi(n + 1)
                        elif job == HT and not (first and par == 0):
                            copy_x_gate(HT, n, par)
                        elif job in (RT, ZT) and not (last and par == 1):
                            copy_x_gate(job, n + 1, 1 - par)
                        elif job == "states_hi" and not (first and par == 0):
                            copy_states_hi(n - 1, 1 - par)
                        elif job == "residual":
                            put_residual(i, n, par, first)
                    for h, (a, b) in enumerate(PARTS):
                        act.wait_ge(pre_summed[R], t * NP + h + 1)
                        nc.scalar.activation(r_gate[:, a:b], pre_sum[R][:, a:b], ACT.Sigmoid).then_inc(r_ready, 1)
                    act.wait_ge(pre_summed[Z], t + 1)
                    nc.scalar.activation(z_gate[:], pre_sum[Z][:], ACT.Sigmoid).then_inc(z_ready, 1)
                    nc.scalar.activation(z_not[:], pre_sum[Z][:], ACT.Sigmoid, scale=-1.0).then_inc(z_not_ready, 1)
                    for h, (a, b) in enumerate(PARTS):
                        act.wait_ge(pre_summed[H], t * NP + h + 1)
                        nc.scalar.activation(cand[:, a:b], pre_sum[H][:, a:b], ACT.Tanh).then_inc(cand_ready, 1)
                    if step == 0 and not (first and par == 0):
                        if not first:
                            act.wait_ge(states_lo_ready, n - 1)
                    act.wait_ge(state_ready, (t + 2) * NP)
                    nc.scalar.copy(states[:, par, :, :, step], state[:]).then_inc(state_kept, 1)

            copy_x_hi(0)
            for g in (R, Z, H):
                copy_x_gate(RT + g, 0, 0)
            copy_x_hi(1)
            tile_loop(act, tile)
            copy_states_hi(tiles - 1, 1)

        @block.vector
        def _(dve):
            nc.vector.memset(ones[:], 1.0)
            nc.vector.memset(bq_mov[:], 0.0).then_inc(bq_ready, 1)
            for n in range(len(mats) * G):
                mat, m = divmod(n, G)
                if mat < n_split:
                    dve.wait_ge(w_hi_ready, n + 1)
                    nc.vector.tensor_tensor(w_split[LO][:, mat, m, :], banks[n % 8][:],
                                            w_split[HI][:, mat, m, :].bitcast(F32), ALU.subtract
                                            ).then_inc(bank_free[n % 8], 1)
                elif n % 2 == 0:
                    dve.wait_ge(w_turned, n + 1)
                    nc.vector.tensor_copy(
                        w_gate[:, mat - n_split, m, :].rearrange("p (j m i) -> p j m i", j=G, m=G),
                        by_block(banks[n % 8][:])).then_inc(bank_free[n % 8], 1)
            dve.wait_ge(bq_loaded, 3 * 16)
            nc.vector.tensor_copy(bq_part[:, 0], bq_raw[:]).then_inc(bq_step, 1)
            dve.wait_ge(bq_step, 1)
            nc.vector.tensor_tensor(bq_rest[:], bq_raw[:], bq_part[:, 0], ALU.subtract).then_inc(bq_step, 1)
            dve.wait_ge(bq_step, 2)
            nc.vector.tensor_copy(bq_part[:, 1], bq_rest[:]).then_inc(bq_step, 1)
            dve.wait_ge(bq_step, 3)
            nc.vector.tensor_tensor(bq_part[:, 2], bq_rest[:], bq_part[:, 1], ALU.subtract).then_inc(bq_step, 1)
            dve.wait_ge(bq_step, 4)
            dve.wait_ge(bq_ready, 1)
            for a in range(3):
                nc.vector.tensor_copy(bq_mov[Q * a:Q * a + 1], bq_part[Q * a:Q * a + 1, a]).then_inc(bq_ready, 1)
            dve.wait_ge(bias_loaded, 6 * 16)
            for g in range(3):
                nc.vector.tensor_tensor(bias_gate[:, g], bias_gate[:, g], bias_raw[:, g], ALU.add
                                        ).then_inc(bias_ready, 1)
            dve.wait_ge(h0_loaded, G * 16)
            nc.vector.transpose(pre_t[R][:], by_block(h0_in[:])).then_inc(h0_turned, 1)
            dve.wait_ge(h0_turned, 1)
            for a, b in PARTS:
                nc.vector.tensor_copy(state[:, a:b], pre_t[R][:, a:b, 0:B]).then_inc(state_ready, 1)

            def take_x_lo(n):
                dve.wait_ge(x_hi_ready, n + 1)
                nc.vector.tensor_tensor(x_part[LO][:].rearrange("p m c -> p (m c)"), job_bank[JOB_BANK[T]][:],
                                        x_part[HI][:].rearrange("p m c -> p (m c)").bitcast(F32), ALU.subtract
                                        ).then_inc(job_copied[T], 1)

            def take_states_lo(n, par):
                dve.wait_ge(states_hi_ready, n + 1)
                nc.vector.tensor_tensor(states_part[LO][:].rearrange("p m c -> p (m c)"),
                                        states[:, par].rearrange("p m b t -> p (m b t)"),
                                        states_part[HI][:].rearrange("p m c -> p (m c)").bitcast(F32),
                                        ALU.subtract).then_inc(states_lo_ready, 1)

            def add_bias(g, n):
                dve.wait_ge(job_done[g], n + 1)
                nc.vector.tensor_tensor(x_rows[:, g, :], job_bank[JOB_BANK[g]][:], bias_gate[:, g, :],
                                        ALU.add).then_inc(job_copied[g], 1)

            def add_residual(n, par):
                dve.wait_ge(job_done[Y], n + 1)
                dve.wait_ge(residual_put, n + 1)
                nc.vector.tensor_tensor(y_out[:, par, :], job_bank[JOB_BANK[Y]][:], y_out[:, par, :], ALU.add
                                        ).then_inc(job_copied[Y], 1)

            def sum_pre(g, t, par, step, parts):
                k = len(parts)
                dve.wait_ge(pre_done[g], t + 1)
                for a, b in parts:
                    nc.vector.transpose(pre_t[g][:, a:b].rearrange("p m b -> p (m b)"),
                                        pre[g][:, Q * a:Q * b]).then_inc(pre_turned[g], 1)
                for h, (a, b) in enumerate(parts):
                    dve.wait_ge(pre_turned[g], t * k + h + 1)
                    nc.vector.tensor_tensor(pre_sum[g][:, a:b], pre_t[g][:, a:b, 0:B],
                                            x_gate[:, par, g, step, a:b], ALU.add).then_inc(pre_summed[g], 1)

            def tile(i, par, first, last):
                n = i * UNROLL + par
                for step in range(TS):
                    t = n * TS + step
                    for job in VECTOR_JOBS.get(step, []):
                        if job == Y and not first:
                            add_residual(n - 2, par)
                        elif job == "x_lo" and not (first and par == 0) and not (last and par == 1):
                            take_x_lo(n + 1)
                        elif job == "states_lo" and not (first and par == 0):
                            take_states_lo(n - 1, 1 - par)
                        elif job in (R, Z, H) and not (last and par == 1):
                            add_bias(job, n + 1)
                    if step == 0:
                        dve.wait_ge(job_copied[ZT], n + 1)
                    sum_pre(R, t, par, step, PARTS)
                    for h, (a, b) in enumerate(PARTS):
                        dve.wait_ge(r_ready, t * NP + h + 1)
                        if h == 0:
                            dve.wait_ge(state_ready, (t + 1) * NP)
                        nc.vector.tensor_tensor(reset_state[:, a:b], r_gate[:, a:b], state[:, a:b], ALU.mult
                                                ).then_inc(reset_ready, 1)
                    sum_pre(Z, t, par, step, [(0, G)])
                    dve.wait_ge(z_ready, t + 1)
                    nc.vector.tensor_tensor(kept[:], z_gate[:], state[:], ALU.mult).then_inc(kept_ready, 1)
                    if step == 0:
                        dve.wait_ge(job_copied[HT], n + 1)
                    sum_pre(H, t, par, step, PARTS)
                    dve.wait_ge(z_not_ready, t + 1)
                    for h, (a, b) in enumerate(PARTS):
                        dve.wait_ge(cand_ready, t * NP + h + 1)
                        nc.vector.tensor_tensor(fresh[:, a:b], z_not[:, a:b], cand[:, a:b], ALU.mult
                                                ).then_inc(fresh_ready, 1)
                    dve.wait_ge(kept_ready, t + 1)
                    if not (first and par == 0 and step == 0):
                        dve.wait_ge(state_kept, t)
                    for h, (a, b) in enumerate(PARTS):
                        dve.wait_ge(fresh_ready, t * NP + h + 1)
                        nc.vector.tensor_tensor(state[:, a:b], fresh[:, a:b], kept[:, a:b], ALU.add
                                                ).then_inc(state_ready, 1)

            take_x_lo(0)
            for g in (R, Z, H):
                dve.wait_ge(bias_ready, g + 1)
                add_bias(g, 0)
            take_x_lo(1)
            tile_loop(dve, tile)
            add_residual(tiles - 2, 0)
            take_states_lo(tiles - 1, 1)
            add_residual(tiles - 1, 1)


_W = "L0_cond_"
_INS = ["x", "cond_1024"] + [_W + n for n in ("Wxr", "Wxz", "Wxh", "bxr", "bxz", "bxh", "Whr", "Whz", "Whh",
                                              "bhr", "bhz", "bhh", "Whq", "bhq")]


def kernel(**inputs):
    import numpy as _np
    import concourse.bacc as _bacc
    from concourse import mybir as _mybir
    from concourse.bass_utils import run_bass_kernel_spmd as _run

    nc = _bacc.Bacc("TRN2", target_bir_lowering=False, num_devices=1)
    arrays, a = {}, {}
    for name in _INS:
        v = _np.ascontiguousarray(inputs[name])
        arrays[f"in_{name}"] = v
        a[name] = nc.dram_tensor(f"in_{name}", v.shape, _mybir.dt.from_np(v.dtype), kind="ExternalInput").ap()
    shape = inputs["x"].shape
    out = nc.dram_tensor("out", shape, _mybir.dt.float32, kind="ExternalOutput").ap()

    def of(kind):
        return [a[f"{_W}{kind}{g}"] for g in "rzh"]

    gru(nc, a["x"], a["cond_1024"], of("Wx"), of("bx"), of("Wh"), of("bh"), a[_W + "Whq"], a[_W + "bhq"], out)
    r = _run(nc, [arrays], core_ids=[0])
    return r.results[0]["out"]
```

```python
from contextlib import ExitStack

import concourse.bass as bass
from concourse import mybir

F32 = mybir.dt.float32
F32R = mybir.dt.float32r
ALU = mybir.AluOpType
ACT = mybir.ActivationFunctionType

P = 128
G = 4
Q = 32
B = 16
TS = 16
ROWS = B * TS
YS = P // B
UNROLL = 2
PARTS = [(0, 1), (1, 2), (2, 4)]
N = len(PARTS)
HI, LO = range(2)
R, Z, H = range(3)
GROUPS = 3 * G
UNITS = [(HI, w, m) for m in range(G) for w in (HI, LO)] + [(LO, HI, m) for m in range(G)]
X_STEP = 2
Y_STEPS = {0: (-1, 0, 6), 1: (-1, 6, 12), 14: (0, 0, 6), 15: (0, 6, 12)}
SCALAR_JOBS = {0: [("states_hi", -1)], 10: [("states_hi", 0)], 14: [("x_hi", 0)], 15: [("x_hi", 1)]}
VECTOR_JOBS = {0: [("x_lo", 1)], 1: [("states_lo", -1)], 2: [("add", -2)], 3: [("add", -1)],
               7: [("residual", 0)], 8: [("residual", 1)], 9: [("x_turn", 0)], 10: [("x_turn", 1)],
               12: [("states_lo", 0)], 15: [("x_lo", 0)]}
SETUP = [("turn", 0), ("turn", 1), ("project", R), ("turn", 2), ("project", Z), ("turn", 3),
         ("project", H), ("turn", 4), ("turn", 5), ("turn", 6)]
SLOTS = 4
TURN_BANKS = 6


def gru(nc, x, h0, w_x, b_x, w_h, b_h, w_q, b_q, out):
    batch, steps, chans = x.shape
    assert batch == B and chans == G * P
    tiles = steps // TS
    turns = tiles // UNROLL
    mats = [*w_x, *w_h, w_q]
    last_mat = len(mats) - 1

    with ExitStack() as ctx:
        def sb(name, shape, dt=F32):
            return ctx.enter_context(nc.sbuf_tensor(name, shape, dt))

        def bank(name):
            return ctx.enter_context(nc.psum_tensor(name, [P, 512], F32))

        def sem(name):
            return ctx.enter_context(nc.semaphore(name))

        w_raw = sb("w_raw", [P, SLOTS, G, chans])
        w_split = [sb(f"w_split{a}", [P, 4, G, chans], F32R) for a in (HI, LO)]
        w_gate = [sb(f"w_gate{g}", [P, G, chans]) for g in range(3)]
        ident = sb("ident", [P, P])
        bias_raw = sb("bias_raw", [P, 3, G])
        bias_gate = sb("bias_gate", [P, 3, G])
        bias_out = sb("bias_out", [P, chans])
        x_in = sb("x_in", [P, B // 2, P])
        x_turned = sb("x_turned", [P, G, ROWS])
        x_part = [sb(f"x_part{a}", [P, G, ROWS], F32R) for a in (HI, LO)]
        x_gate = sb("x_gate", [P, 2, 3, G, B, TS])
        y_out = sb("y_out", [P, 2, chans])
        states = sb("states", [P, 2, G, B, YS])
        states_part = [sb(f"states_part{a}", [P, G, P], F32R) for a in (HI, LO)]
        h0_in = sb("h0_in", [P, P])
        state = sb("state", [P, G, B])
        reset_state = sb("reset_state", [P, G, B])
        pre_t = [sb(f"pre_t{g}", [P, G, Q]) for g in range(3)]
        z_pre = sb("z_pre", [P, G, B])
        r_gate = sb("r_gate", [P, G, B])
        z_gate = sb("z_gate", [P, G, B])
        z_not = sb("z_not", [P, G, B])
        cand = sb("cand", [P, G, B])
        kept = sb("kept", [P, G, B])
        fresh = sb("fresh", [P, G, B])

        pre = [bank(f"pre{g}") for g in range(3)]
        y_bank = [bank(f"y_bank{n}") for n in range(2)]
        spare_bank = bank("spare_bank")
        x_bank = [bank(f"x_bank{n}") for n in range(2)]
        turn_bank = [*pre, *y_bank, spare_bank]

        zeroed = sem("zeroed")
        ident_ready = sem("ident_ready")
        w_loaded = [sem(f"w_loaded{m}") for m in range(len(mats))]
        bias_gate_loaded = sem("bias_gate_loaded")
        bias_out_loaded = sem("bias_out_loaded")
        bias_ready = sem("bias_ready")
        h0_loaded = sem("h0_loaded")
        banks_primed = sem("banks_primed")
        h0_turned = sem("h0_turned")
        w_turned = sem("w_turned")
        w_hi_ready = sem("w_hi_ready")
        bank_free = [sem(f"bank_free{n}") for n in range(TURN_BANKS)]
        x_loaded = sem("x_loaded")
        x_turn_done = sem("x_turn_done")
        x_hi_ready = sem("x_hi_ready")
        x_lo_ready = sem("x_lo_ready")
        x_projected = sem("x_projected")
        x_copied = sem("x_copied")
        residual_loaded = [sem("residual_loaded0"), sem("residual_loaded1")]
        residual_put = sem("residual_put")
        states_hi_ready = sem("states_hi_ready")
        states_lo_ready = sem("states_lo_ready")
        y_projected = sem("y_projected")
        y_copied = sem("y_copied")
        stored = [sem("stored0"), sem("stored1")]
        pre_done = [sem("r_pre_done"), sem("z_pre_done"), sem("h_pre_done")]
        z_pre_summed = sem("z_pre_summed")
        pre_turned = [[sem(f"{g}_pre_turned{h}") for h in range(N)] for g in "rzh"]
        r_ready = [sem(f"r_ready{h}") for h in range(N)]
        z_ready = sem("z_ready")
        cand_ready = [sem(f"cand_ready{h}") for h in range(N)]
        reset_ready = [sem(f"reset_ready{h}") for h in range(N)]
        fresh_ready = [sem(f"fresh_ready{h}") for h in range(N)]
        state_ready = [sem(f"state_ready{h}") for h in range(N)]
        state_kept = sem("state_kept")

        block = ctx.enter_context(nc.Block())


        def by_block(t):
            if t.shape[-1] == P:
                return t.rearrange("p (i m) -> p m i", m=G)
            return t.rearrange("p (j i m) -> p j m i", j=G, m=G)

        def ordered(mat, to, of):
            if mat < 3:
                return to.rearrange("p (m c) -> p m c", m=G), of.rearrange("p (c m) -> p m c", m=G)
            if mat < 6:
                return to.rearrange("p (j m i) -> p j m i", j=G, m=G), by_block(of)
            return to, of

        SPLIT_MATS = [0, 1, 2, last_mat]

        def split_place(mat, a, m):
            return w_split[a][:, mat if mat < 3 else 3, m, :]

        def flat(t):
            return t.rearrange("p m c -> p (m c)")

        out_v = out.rearrange("b (u t) c -> u b t c", t=YS)
        x_res = x.rearrange("b (u t) c -> u b t c", t=YS)
        x_v = x.rearrange("(q s) (n t) (j c) -> n j s t q c", s=2, t=TS, j=G)
        X_LOADS = 2 * G

        def tile_loop(eng, tile):
            for par in range(UNROLL):
                tile(0, par, first=par == 0, second=par == 1, last=False, end=False)
            with eng.Fori(1, turns - 1) as i:
                for par in range(UNROLL):
                    tile(i, par, first=False, last=False, end=False)
            for par in range(UNROLL):
                tile(turns - 1, par, first=False, last=par == 1, end=True)

        @block.sync
        def _(sp):
            def load_x(n):
                for j in range(G):
                    for s in range(2):
                        sp.dma_start(x_in[Q * j + TS * s:Q * j + TS * (s + 1)], x_v[n, j, s]
                                     ).then_inc(x_loaded, 16)

            def load_residual(u, half):
                sp.dma_start(y_out[:, half, :], x_res[u]).then_inc(residual_loaded[half], 16)

            def store(u, half):
                sp.dma_start(out_v[u], y_out[:, half, :]).then_inc(stored[half], 16)

            def tile(i, par, first, last, end, second=False):
                n = i * UNROLL + par
                if not end:
                    sp.wait_ge(x_turn_done, 2 * n + 4)
                    load_x(n + 2)
                if not first:
                    for half in range(2):
                        sp.wait_ge(y_copied, 2 * n - 1 + half)
                        store(2 * n - 2 + half, half)
                    for half in range(2):
                        sp.wait_ge(stored[half], n * 16)
                        load_residual(2 * n + half, half)

            def load_mat(mat):
                if mat >= SLOTS:
                    sp.wait_ge(w_turned, (mat - SLOTS + 1) * G)
                sp.dma_start(w_raw[:, mat % SLOTS], mats[mat].rearrange("(j n) c -> n j c", j=G)
                             ).then_inc(w_loaded[mat], 16)

            load_mat(0)
            load_x(0)
            load_mat(1)
            load_mat(2)
            for a, b in enumerate((b_x, b_h)):
                for g in range(3):
                    sp.dma_start((bias_gate if a == 0 else bias_raw)[:, g, :],
                                 b[g].rearrange("(c m) -> c m", m=G)).then_inc(bias_gate_loaded, 16)
            load_mat(3)
            sp.wait_ge(zeroed, 1)
            for j in range(G):
                sp.dma_start(h0_in[Q * j:Q * j + B, :], h0[:, P * j:P * (j + 1)]).then_inc(h0_loaded, 16)
            load_mat(4)
            sp.wait_ge(x_turn_done, 2)
            load_x(1)
            load_mat(5)
            load_mat(6)
            sp.dma_start(bias_out[:], b_q.rearrange("(a n) -> a n", a=1).to_broadcast([P, chans])
                         ).then_inc(bias_out_loaded, 16)
            for half in range(2):
                load_residual(half, half)
            tile_loop(sp, tile)
            for half in range(2):
                sp.wait_ge(y_copied, 2 * tiles - 1 + half)
                store(2 * tiles - 2 + half, half)
            for half in range(2):
                sp.wait_ge(stored[half], tiles * 16)

        @block.gpsimd
        def _(pool):
            nc.gpsimd.memset(ident[:], 0.0).then_inc(ident_ready, 1)
            pool.wait_ge(ident_ready, 1)
            nc.gpsimd.affine_select(out=ident[:], in_=ident[:], compare_op=ALU.not_equal, fill=1.0,
                                    base=0, pattern=[[-1, P]], channel_multiplier=1
                                    ).then_inc(ident_ready, 1)
            nc.gpsimd.memset(h0_in[:], 0.0).then_inc(zeroed, 1)

        @block.tensor
        def _(pe):
            def turn_mat(mat):
                pe.wait_ge(w_loaded[mat], 16)
                for m in range(G):
                    n = mat * G + m
                    if n >= TURN_BANKS:
                        pe.wait_ge(bank_free[n % TURN_BANKS], n // TURN_BANKS)
                    for j in range(G):
                        mm = nc.tensor.transpose(
                            turn_bank[n % TURN_BANKS][:, P * j:P * (j + 1)],
                            w_raw[:, mat % SLOTS, j, :].rearrange("p (c m) -> p m c", m=G)[:, m, :], ident[:])
                    mm.then_inc(w_turned, 1)

            def wait_for_mats(mat):
                for n in range(TURN_BANKS):
                    pe.wait_ge(bank_free[n], (mat * G + G - 1 - n) // TURN_BANKS + 1)

            def project_x(d, k, unused_bank=False):
                g, m_out = divmod(k, G)
                if not unused_bank:
                    pe.wait_ge(x_copied, d * GROUPS + k - 1)
                for u, (a, w, m) in enumerate(UNITS):
                    mm = nc.tensor.matmul(x_bank[k % 2][:, 0:ROWS], w_split[w][:, g, m, P * m_out:P * (m_out + 1)],
                                          x_part[a][:, m, :], start=(u == 0), stop=(u == len(UNITS) - 1))
                mm.then_inc(x_projected, 1)

            def project_states(u, half, first_unit, stop):
                for k in range(first_unit, stop):
                    a, w, m = UNITS[k]
                    if k == 0:
                        pe.wait_ge(states_hi_ready, u + 1)
                    if (a, m) == (LO, 0):
                        pe.wait_ge(states_lo_ready, u + 1)
                    mm = nc.tensor.matmul(y_bank[half][:], states_part[a][:, m, :], w_split[w][:, 3, m, :],
                                          start=(k == 0), stop=(k == len(UNITS) - 1))
                if stop == len(UNITS):
                    mm.then_inc(y_projected, 1)

            def recur(g, t):
                for m in range(G):
                    for h, (a, _) in enumerate(PARTS):
                        if m == a and g == R:
                            pe.wait_ge(state_ready[h], t + 1)
                        if m == a and g == H:
                            pe.wait_ge(reset_ready[h], t + 1)
                    of = reset_state if g == H else state
                    for j in range(G):
                        mm = nc.tensor.matmul(pre[g][Q * j:Q * j + B, 0:P], of[:, m, :],
                                              w_gate[g][:, m, P * j:P * (j + 1)],
                                              start=(g == Z and m == 0), stop=(m == G - 1),
                                              skip_group_check=(g != Z))
                mm.then_inc(pre_done[g], 1)

            def tile(i, par, first, last, end, second=False):
                n = i * UNROLL + par
                for step in range(TS):
                    t = n * TS + step
                    recur(R, t)
                    recur(Z, t)
                    recur(H, t)
                    if X_STEP <= step < X_STEP + GROUPS and not last:
                        if step == X_STEP:
                            pe.wait_ge(x_lo_ready, 2 * n + 4)
                        project_x(n + 1, step - X_STEP)
                    if step in Y_STEPS:
                        half, first_unit, stop = Y_STEPS[step]
                        if not (first and half < 0):
                            if first_unit == 0 and not (first or half < 0 and second):
                                pe.wait_ge(y_copied, 2 * n + half - 1)
                            project_states(2 * n + half, half % 2, first_unit, stop)

            pe.wait_ge(ident_ready, 2)
            for what, k in SETUP:
                if what == "turn":
                    turn_mat(k)
                else:
                    if k == R:
                        pe.wait_ge(x_lo_ready, 2)
                    wait_for_mats(k)
                    for m_out in range(G):
                        project_x(0, k * G + m_out, unused_bank=k * G + m_out < 2)
            wait_for_mats(last_mat)
            for g in (R, H):
                for j in range(G):
                    mm = nc.tensor.matmul(pre[g][Q * j:Q * j + B, 0:P], ident[:, 0:B], ident[:],
                                          start=True, stop=True)
            mm.then_inc(banks_primed, 1)
            tile_loop(pe, tile)
            project_states(2 * tiles - 1, 1, 0, len(UNITS))

        @block.scalar
        def _(act):
            def copy_mat(mat):
                for m in range(G):
                    n = mat * G + m
                    of = turn_bank[n % TURN_BANKS]
                    if mat in SPLIT_MATS:
                        act.wait_ge(w_turned, n + 1)
                        to, of = ordered(mat, split_place(mat, HI, m), of[:])
                        nc.scalar.copy(to, of).then_inc(w_hi_ready, 1)
                    elif m % 2:
                        act.wait_ge(w_turned, n + 1)
                        to, of = ordered(mat, w_gate[mat - 3][:, m, :], of[:])
                        nc.scalar.copy(to, of).then_inc(bank_free[n % TURN_BANKS], 1)

            def copy_x_hi(d, half, is_first=False):
                act.wait_ge(x_turn_done, 2 * d + half + 1)
                if not is_first:
                    act.wait_ge(x_projected, d * GROUPS)
                ms = slice(2 * half, 2 * half + 2)
                nc.scalar.copy(flat(x_part[HI][:, ms]), flat(x_turned[:, ms])).then_inc(x_hi_ready, 1)

            def copy_x_gate(d, k, par):
                g, m_out = divmod(k, G)
                act.wait_ge(x_projected, d * GROUPS + k + 1)
                nc.scalar.activation(x_gate[:, par, g, m_out].rearrange("p b t -> p (b t)"),
                                     x_bank[k % 2][:, 0:ROWS], ACT.Identity,
                                     bias=bias_gate[:, g, m_out:m_out + 1]).then_inc(x_copied, 1)

            def copy_states_hi(u, half, first):
                act.wait_ge(state_kept, (u + 1) * YS)
                if not first:
                    act.wait_ge(y_projected, u)
                nc.scalar.copy(flat(states_part[HI][:]), states[:, half].rearrange("p m b t -> p (m b t)")
                               ).then_inc(states_hi_ready, 1)

            def tile(i, par, first, last, end, second=False):
                n = i * UNROLL + par
                for step in range(TS):
                    t = n * TS + step
                    if X_STEP < step <= X_STEP + GROUPS and not last:
                        copy_x_gate(n + 1, step - X_STEP - 1, 1 - par)
                    if first and step == 0:
                        for half in range(2):
                            copy_x_hi(1, half)
                    for job, half in SCALAR_JOBS.get(step, []):
                        if job == "states_hi" and not (first and half < 0):
                            copy_states_hi(2 * n + half, half % 2, first)
                        elif job == "x_hi" and not end:
                            copy_x_hi(n + 2, half)
                    for h, (a, b) in enumerate(PARTS):
                        act.wait_ge(pre_turned[R][h], t + 1)
                        nc.scalar.activation(r_gate[:, a:b], pre_t[R][:, a:b, 0:B], ACT.Sigmoid).then_inc(r_ready[h], 1)
                    act.wait_ge(z_pre_summed, t + 1)
                    nc.scalar.activation(z_gate[:], z_pre[:], ACT.Sigmoid).then_inc(z_ready, 1)
                    nc.scalar.activation(z_not[:], z_pre[:], ACT.Sigmoid, scale=-1.0)
                    for h, (a, b) in enumerate(PARTS):
                        act.wait_ge(pre_turned[H][h], t + 1)
                        nc.scalar.activation(cand[:, a:b], pre_t[H][:, a:b, 0:B], ACT.Tanh
                                             ).then_inc(cand_ready[h], 1)
                    if step % YS == 0 and not first:
                        act.wait_ge(states_lo_ready, 2 * n + step // YS - 1)
                    act.wait_ge(state_ready[N - 1], t + 2)
                    nc.scalar.copy(states[:, step // YS, :, :, step % YS], state[:]).then_inc(state_kept, 1)

            for half in range(2):
                copy_x_hi(0, half, is_first=True)
            for what, k in SETUP:
                if what == "turn":
                    copy_mat(k)
                else:
                    act.wait_ge(bias_ready, 1)
                    for m_out in range(G):
                        copy_x_gate(0, k * G + m_out, 0)
            tile_loop(act, tile)
            copy_states_hi(2 * tiles - 1, 1, False)

        @block.vector
        def _(dve):
            def take_mat(mat):
                for m in range(G):
                    n = mat * G + m
                    of = turn_bank[n % TURN_BANKS]
                    if mat in SPLIT_MATS:
                        dve.wait_ge(w_hi_ready, SPLIT_MATS.index(mat) * G + m + 1)
                        to, pre_of = ordered(mat, split_place(mat, LO, m), of[:])
                        hi, _ = ordered(mat, split_place(mat, HI, m).bitcast(F32), of[:])
                        nc.vector.tensor_tensor(to, pre_of, hi, ALU.subtract).then_inc(bank_free[n % TURN_BANKS], 1)
                    elif m % 2 == 0:
                        dve.wait_ge(w_turned, n + 1)
                        to, of = ordered(mat, w_gate[mat - 3][:, m, :], of[:])
                        nc.vector.tensor_copy(to, of).then_inc(bank_free[n % TURN_BANKS], 1)

            def turn_x(d, half, is_first=False):
                if half == 0:
                    dve.wait_ge(x_loaded, (d + 1) * X_LOADS * 16)
                    if not is_first:
                        dve.wait_ge(x_lo_ready, 2 * d)
                ms = slice(2 * half, 2 * half + 2)
                nc.vector.transpose(x_turned[:, ms].rearrange("p m (q r) -> p m q r", r=Q),
                                    x_in[:].rearrange("p q (i m) -> p m q i", m=G)[:, ms]).then_inc(x_turn_done, 1)

            def take_x_lo(d, half):
                dve.wait_ge(x_hi_ready, 2 * d + half + 1)
                ms = slice(2 * half, 2 * half + 2)
                nc.vector.tensor_tensor(flat(x_part[LO][:, ms]), flat(x_turned[:, ms]),
                                        flat(x_part[HI][:, ms]).bitcast(F32), ALU.subtract
                                        ).then_inc(x_lo_ready, 1)

            def take_states_lo(u, half):
                dve.wait_ge(states_hi_ready, u + 1)
                nc.vector.tensor_tensor(flat(states_part[LO][:]), states[:, half].rearrange("p m b t -> p (m b t)"),
                                        flat(states_part[HI][:]).bitcast(F32), ALU.subtract
                                        ).then_inc(states_lo_ready, 1)

            def put_residual(n, half):
                dve.wait_ge(residual_loaded[half], (n + 1) * 16)
                nc.vector.tensor_tensor(y_out[:, half, :], y_out[:, half, :], bias_out[:], ALU.add
                                        ).then_inc(residual_put, 1)

            def add_residual(u, half):
                dve.wait_ge(y_projected, u + 1)
                dve.wait_ge(residual_put, u + 1)
                nc.vector.tensor_tensor(y_out[:, half, :], y_bank[half][:], y_out[:, half, :], ALU.add
                                        ).then_inc(y_copied, 1)

            def turn_pre(g, t, h):
                a, b = PARTS[h]
                if h == 0:
                    dve.wait_ge(pre_done[g], t + 1)
                nc.vector.transpose(pre_t[g][:, a:b].rearrange("p m b -> p (m b)"), pre[g][:, Q * a:Q * b]
                                    ).then_inc(pre_turned[g][h], 1)

            def put_x(g, par, step):
                rows = x_gate[:, par, g, :, :, step:step + 1].rearrange("p m b s -> p m s b")
                nc.vector.transpose(pre[g][:, 0:P].rearrange("p (m i) -> p m i", m=G),
                                    rows.to_broadcast([P, G, 2, B]))

            def reset(t, h):
                a, b = PARTS[h]
                dve.wait_ge(r_ready[h], t + 1)
                nc.vector.tensor_tensor(reset_state[:, a:b], r_gate[:, a:b], state[:, a:b],
                                        ALU.mult).then_inc(reset_ready[h], 1)

            def take_fresh(t, h):
                a, b = PARTS[h]
                dve.wait_ge(cand_ready[h], t + 1)
                nc.vector.tensor_tensor(fresh[:, a:b], z_not[:, a:b], cand[:, a:b], ALU.mult
                                        ).then_inc(fresh_ready[h], 1)

            def renew(t, h):
                a, b = PARTS[h]
                dve.wait_ge(fresh_ready[h], t + 1)
                nc.vector.tensor_tensor(state[:, a:b], fresh[:, a:b], kept[:, a:b], ALU.add
                                        ).then_inc(state_ready[h], 1)

            def tile(i, par, first, last, end, second=False):
                n = i * UNROLL + par
                for step in range(TS):
                    t = n * TS + step
                    if first and 0 < step <= 2:
                        take_x_lo(1, step - 1)
                    for job, k in VECTOR_JOBS.get(step, []):
                        if job == "x_turn" and not end:
                            turn_x(n + 2, k)
                        elif job == "x_lo" and k == 0 and not end:
                            take_x_lo(n + 2, k)
                        elif job == "x_lo" and k == 1 and not first and not last:
                            take_x_lo(n + 1, k)
                        elif job == "residual":
                            put_residual(n, k)
                        elif job == "add" and not first:
                            add_residual(2 * n + k, k % 2)
                        elif job == "states_lo" and not (first and k < 0):
                            take_states_lo(2 * n + k, k % 2)
                    for h in range(N):
                        turn_pre(R, t, h)
                    put_x(H, par, step)
                    for h in range(N):
                        reset(t, h)
                    dve.wait_ge(pre_done[Z], t + 1)
                    nc.vector.transpose(flat(pre_t[Z][:]), pre[Z][:, 0:P]).then_inc(pre_turned[Z][0], 1)
                    dve.wait_ge(pre_turned[Z][0], t + 1)
                    nc.vector.tensor_tensor(z_pre[:], pre_t[Z][:, :, 0:B], x_gate[:, par, Z, :, :, step],
                                            ALU.add).then_inc(z_pre_summed, 1)
                    for h in range(N):
                        turn_pre(H, t, h)
                    dve.wait_ge(z_ready, t + 1)
                    nc.vector.tensor_tensor(kept[:], z_gate[:], state[:], ALU.mult)
                    take_fresh(t, 0)
                    if step < TS - 1:
                        put_x(R, par, step + 1)
                    elif not last:
                        dve.wait_ge(x_copied, (n + 2) * GROUPS)
                        put_x(R, 1 - par, 0)
                    renew(t, 0)
                    take_fresh(t, 1)
                    take_fresh(t, 2)
                    renew(t, 1)
                    renew(t, 2)

            for half in range(2):
                turn_x(0, half, is_first=True)
            for half in range(2):
                take_x_lo(0, half)
            for what, k in SETUP:
                if what == "turn":
                    take_mat(k)
                elif k == R:
                    dve.wait_ge(bias_gate_loaded, 6 * 16)
                    nc.vector.tensor_tensor(flat(bias_gate[:]), flat(bias_gate[:]), flat(bias_raw[:]), ALU.add
                                            ).then_inc(bias_ready, 1)
                elif k == H:
                    for half in range(2):
                        turn_x(1, half)
            dve.wait_ge(h0_loaded, G * 16)
            nc.vector.transpose(pre_t[R][:], by_block(h0_in[:])).then_inc(h0_turned, 1)
            dve.wait_ge(h0_turned, 1)
            dve.wait_ge(x_copied, GROUPS)
            dve.wait_ge(banks_primed, 1)
            put_x(R, 0, 0)
            for h, (a, b) in enumerate(PARTS):
                nc.vector.tensor_copy(state[:, a:b], pre_t[R][:, a:b, 0:B]).then_inc(state_ready[h], 1)
            dve.wait_ge(bias_out_loaded, 16)
            tile_loop(dve, tile)
            for half in range(2):
                if half == 1:
                    take_states_lo(2 * tiles - 1, 1)
                add_residual(2 * tiles - 2 + half, half)


_W = "L0_cond_"
_INS = ["x", "cond_1024"] + [_W + n for n in ("Wxr", "Wxz", "Wxh", "bxr", "bxz", "bxh", "Whr", "Whz", "Whh",
                                              "bhr", "bhz", "bhh", "Whq", "bhq")]


def kernel(**inputs):
    import numpy as _np
    import concourse.bacc as _bacc
    from concourse import mybir as _mybir
    from concourse.bass_utils import run_bass_kernel_spmd as _run

    nc = _bacc.Bacc("TRN2", target_bir_lowering=False, num_devices=1)
    arrays, a = {}, {}
    for name in _INS:
        v = _np.ascontiguousarray(inputs[name])
        arrays[f"in_{name}"] = v
        a[name] = nc.dram_tensor(f"in_{name}", v.shape, _mybir.dt.from_np(v.dtype), kind="ExternalInput").ap()
    shape = inputs["x"].shape
    out = nc.dram_tensor("out", shape, _mybir.dt.float32, kind="ExternalOutput").ap()

    def of(kind):
        return [a[f"{_W}{kind}{g}"] for g in "rzh"]

    gru(nc, a["x"], a["cond_1024"], of("Wx"), of("bx"), of("Wh"), of("bh"), a[_W + "Whq"], a[_W + "bhq"], out)
    r = _run(nc, [arrays], core_ids=[0])
    return r.results[0]["out"]
```
